# Optimizing a Trainium2 kernel written in Bass

```python
import numpy as np
import jax
import jax.numpy as jnp

def _softmax(x, axis=-1):
    return jax.nn.softmax(x, axis=axis)

def _gelu(x):
    return jax.nn.gelu(x, approximate=True)

def _silu(x):
    return jax.nn.silu(x)

def _sigmoid(x):
    return jax.nn.sigmoid(x)

def _layernorm(x, axis=-1, eps=1e-05):
    m = jnp.mean(x, axis=axis, keepdims=True)
    v = jnp.var(x, axis=axis, keepdims=True)
    return (x - m) / jnp.sqrt(v + eps)

def _scatter_add(tgt, idx, src, axis=0):
    return tgt.at[idx].add(src)

def _segment_sum(src, seg, n):
    return jax.ops.segment_sum(src, seg, n)
kernel_name = 'mk_macaron_d1_jaxref_r8_17b66c'

def setup_inputs(seed: int=0):
    np.random.seed(seed)
    _w = jnp.asarray

    def _L0_attn_setup():
        import jax, jax.numpy as jnp
        import numpy as np
        B, S, H = (16, 64, 256)
        NH, NKV = (16, 4)
        HD = H // NH

        def _rope_tables(seq_len, dim, dtype):
            inv_freq = 1.0 / 10000.0 ** (jnp.arange(0, dim, 2, dtype=jnp.float32) / dim)
            t = jnp.arange(seq_len, dtype=jnp.float32)
            freqs = jnp.einsum('i,j->ij', t, inv_freq)
            emb = jnp.concatenate([freqs, freqs], axis=-1)
            cos = jnp.cos(emb)[None, None].astype(dtype)
            sin = jnp.sin(emb)[None, None].astype(dtype)
            return (cos, sin)

        def _rotate_half(x):
            x1, x2 = jnp.split(x, 2, axis=-1)
            return jnp.concatenate([-x2, x1], axis=-1)
        key = jax.random.key(seed)
        kx, kq, kk, kv, ko = jax.random.split(key, 5)
        x = jax.random.normal(kx, (B, S, H), dtype=jnp.float32)
        s = 0.02
        Wq = jax.random.normal(kq, (H, H), dtype=jnp.float32) * s
        Wk = jax.random.normal(kk, (NKV * HD, H), dtype=jnp.float32) * s
        Wv = jax.random.normal(kv, (NKV * HD, H), dtype=jnp.float32) * s
        Wo = jax.random.normal(ko, (H, H), dtype=jnp.float32) * s
        return {'x': x, 'Wq': Wq, 'Wk': Wk, 'Wv': Wv, 'Wo': Wo}
    _L0_attn_in = _L0_attn_setup()

    def _L0_ffn_setup():
        import jax, jax.numpy as jnp
        import numpy as np
        NUM_EXPERTS = 32
        TOP_K = 8
        THRESHOLD = 0.8
        HIDDEN = 256
        INTER = 96
        key = jax.random.key(seed)
        k1, k2, k3, k4 = jax.random.split(key, 4)
        hidden_states = jax.random.normal(k1, (2, 128, HIDDEN), jnp.float32)
        gate_weight = jax.random.normal(k2, (NUM_EXPERTS, HIDDEN), jnp.float32) * 0.02
        gate_up_proj = jax.random.normal(k3, (NUM_EXPERTS, 2 * INTER, HIDDEN), jnp.float32) * 0.02
        down_proj = jax.random.normal(k4, (NUM_EXPERTS, HIDDEN, INTER), jnp.float32) * 0.02
        return {'hidden_states': hidden_states, 'gate_weight': gate_weight, 'gate_up_proj': gate_up_proj, 'down_proj': down_proj}
    _L0_ffn_in = _L0_ffn_setup()
    _d = {'L0_attn_x': _L0_attn_in['x'], 'L0_attn_Wq': _L0_attn_in['Wq'], 'L0_attn_Wk': _L0_attn_in['Wk'], 'L0_attn_Wv': _L0_attn_in['Wv'], 'L0_attn_Wo': _L0_attn_in['Wo'], 'L0_ffn_gate_weight': _L0_ffn_in['gate_weight'], 'L0_ffn_gate_up_proj': _L0_ffn_in['gate_up_proj'], 'L0_ffn_down_proj': _L0_ffn_in['down_proj']}
    _x0 = _d['L0_attn_x']
    _d['L0_attn_x'] = jax.random.normal(jax.random.fold_in(jax.random.key(seed), 1), (4, 1024, 256), dtype=_x0.dtype)
    del _x0
    return _d

def reference(L0_attn_x, L0_attn_Wq, L0_attn_Wk, L0_attn_Wv, L0_attn_Wo, L0_ffn_gate_weight, L0_ffn_gate_up_proj, L0_ffn_down_proj):

    def _L0_attn_ref(x, Wq, Wk, Wv, Wo):
        import jax, jax.numpy as jnp
        import numpy as np
        B, S, H = (16, 64, 256)
        NH, NKV = (16, 4)
        HD = H // NH

        def _rope_tables(seq_len, dim, dtype):
            inv_freq = 1.0 / 10000.0 ** (jnp.arange(0, dim, 2, dtype=jnp.float32) / dim)
            t = jnp.arange(seq_len, dtype=jnp.float32)
            freqs = jnp.einsum('i,j->ij', t, inv_freq)
            emb = jnp.concatenate([freqs, freqs], axis=-1)
            cos = jnp.cos(emb)[None, None].astype(dtype)
            sin = jnp.sin(emb)[None, None].astype(dtype)
            return (cos, sin)

        def _rotate_half(x):
            x1, x2 = jnp.split(x, 2, axis=-1)
            return jnp.concatenate([-x2, x1], axis=-1)
        b, s, _ = x.shape
        scaling = HD ** (-0.5)
        q = jnp.einsum('bsh,oh->bso', x, Wq).reshape(b, s, NH, HD).transpose(0, 2, 1, 3)
        k = jnp.einsum('bsh,oh->bso', x, Wk).reshape(b, s, NKV, HD).transpose(0, 2, 1, 3)
        v = jnp.einsum('bsh,oh->bso', x, Wv).reshape(b, s, NKV, HD).transpose(0, 2, 1, 3)
        cos, sin = _rope_tables(s, HD, x.dtype)
        q = q * cos + _rotate_half(q) * sin
        k = k * cos + _rotate_half(k) * sin
        rep = NH // NKV
        k = jnp.repeat(k, rep, axis=1)
        v = jnp.repeat(v, rep, axis=1)
        scores = jnp.einsum('bhqd,bhkd->bhqk', q, k) * scaling
        attn = jax.nn.softmax(scores, axis=-1)
        out = jnp.einsum('bhqk,bhkd->bhqd', attn, v)
        out = out.transpose(0, 2, 1, 3).reshape(b, s, H)
        return jnp.einsum('bsh,oh->bso', out, Wo)

    def _L0_ffn_ref(hidden_states, gate_weight, gate_up_proj, down_proj):
        import jax, jax.numpy as jnp
        import numpy as np
        NUM_EXPERTS = 32
        TOP_K = 8
        THRESHOLD = 0.8
        HIDDEN = 256
        INTER = 96
        B, S, H = hidden_states.shape
        x = hidden_states.reshape(-1, H)
        logits = x @ gate_weight.T
        probs = jax.nn.softmax(logits.astype(jnp.float32), axis=-1).astype(logits.dtype)
        top_vals, top_idx = jax.lax.top_k(probs, TOP_K)
        renorm = top_vals / jnp.clip(jnp.sum(top_vals, axis=-1, keepdims=True), 1e-12)
        cum = jnp.cumsum(renorm, axis=-1)
        num_keep = jnp.minimum(jnp.sum((cum < THRESHOLD).astype(jnp.int32), axis=-1) + 1, TOP_K)
        active = jnp.arange(TOP_K)[None, :] < num_keep[:, None]
        rw = top_vals * active.astype(top_vals.dtype)
        rw = rw / jnp.clip(jnp.sum(rw, axis=-1, keepdims=True), 1e-12)
        combine = jnp.sum(jax.nn.one_hot(top_idx, NUM_EXPERTS, dtype=rw.dtype) * rw[..., None], axis=1)

        def body(acc, params):
            w_gu, w_d, ce = params
            gu = x @ w_gu.T
            g, u = jnp.split(gu, 2, axis=-1)
            h = jax.nn.silu(g) * u
            return (acc + h @ w_d.T * ce[:, None], None)
        out, _ = jax.lax.scan(body, jnp.zeros_like(x), (gate_up_proj, down_proj, combine.T))
        return out.reshape(B, S, H)
    x = L0_attn_x
    x = x + 0.5 * _L0_ffn_ref(_layernorm(x, axis=-1), L0_ffn_gate_weight, L0_ffn_gate_up_proj, L0_ffn_down_proj)
    x = x + _L0_attn_ref(_layernorm(x, axis=-1), L0_attn_Wq, L0_attn_Wk, L0_attn_Wv, L0_attn_Wo)
    x = x + 0.5 * _L0_ffn_ref(_layernorm(x, axis=-1), L0_ffn_gate_weight, L0_ffn_gate_up_proj, L0_ffn_down_proj)
    return x

_drawn_inputs = setup_inputs


def setup_inputs(seed=0):
    import zlib

    import numpy as np

    out = dict(_drawn_inputs(seed))
    spreads = {}
    factors = {'L0_attn_Wq': 8.0,
     'L0_attn_Wk': 8.0,
     'L0_attn_Wv': 8.0,
     'L0_attn_Wo': 8.0,
     'L0_ffn_gate_weight': 8.0,
     'L0_ffn_gate_up_proj': 8.0,
     'L0_ffn_down_proj': 8.0}
    for name, (base, spread) in spreads.items():
        noise = np.random.default_rng([zlib.crc32(name.encode()), seed]).standard_normal(out[name].shape)
        drawn = base * np.exp(spread * noise) if base else spread * noise
        out[name] = jnp.asarray(drawn.astype(out[name].dtype))
    for name, factor in factors.items():
        out[name] = (out[name] * factor).astype(out[name].dtype)
    return out
```

```python
from contextlib import ExitStack

import numpy as np

import concourse.bass as bass
from concourse import mybir

ALU = mybir.AluOpType
ACT = mybir.ActivationFunctionType
F32 = mybir.dt.float32
F16 = mybir.dt.float16
I32 = mybir.dt.int32
AX_X = mybir.AxisListType.X
ABSMAX = bass.bass_isa.ReduceOp.max

P = 128
BATCH, SEQ, HID = 4, 1024, 256
TOKENS = BATCH * SEQ
KT = HID // P
TILES = TOKENS // P
GT = 4
GROUP = GT * P
GROUPS = TOKENS // GROUP
EXPERTS, TOPK, INTER = 32, 8, 96
CHUNKS = EXPERTS * INTER // P
HEADS, KV, HD = 16, 4, 16
REP = HEADS // KV
UNITS = BATCH * KV
QT = SEQ // P
ROPE_LINKS = 3 * KV + 4
KEEP_BELOW = 0.8
EPS = 1e-5

X_UP = 2.0 ** 8
W_UP = 2.0 ** 12
C_UP = 2.0 ** 12
XW = X_UP * W_UP
M_UNIT = 2.0 ** 15

S_GU, S_D, S_G, S_Q, S_K, S_V, S_O = range(7)
N_SCALES = 8
B_Y, B_G, B_U, B_C, B_PREP = 0, 2, 4, 6, 7
B_MAX, B_EXP, B_OUT = 0, 2, 6
N0_DVE, N0_T_HI, N0_T_LO, LOGITS = range(0, 5), 6, 7, 8
R_DVE, R_EXP, R_T = range(9, 17), 10, 18
N1_DVE, N1_T_HI, N1_T_LO = range(5, 10), 11, 12
J_AT = (13, 14, 15, 16, 19, 20, 21)
MAX_FROM, MAX_TO = 4, 29
LAG = 3
NP_BUF = 4


def max_parts(step, quarter):
    begun = lambda n: max(0, min(64, 64 * (n - 4 * MAX_FROM) // (4 * (MAX_TO - MAX_FROM))))
    n = 4 * step + quarter
    return range(begun(n), begun(n + 1))


def build(nc, x, wgu, wd, wg, wq, wk, wv, wo, sel_c, ident_c, qtab_c, ktab_c, out):
    with ExitStack() as ctx:
        def sb(name, shape, dt=F32):
            return ctx.enter_context(nc.sbuf_tensor(name, shape, dt))

        def sem(name):
            return ctx.enter_context(nc.semaphore(name))

        X = sb("X", [P, TILES, HID])
        WGU = [sb(f"WGU{h}", [P, KT, 2 * CHUNKS, P], F16) for h in range(2)]
        WD = [sb(f"WD{h}", [P, CHUNKS, HID], F16) for h in range(2)]
        WG = [sb(f"WG{h}", [P, KT, EXPERTS], F16) for h in range(2)]
        WQ = [sb(f"WQ{h}", [P, KT, KV, P], F16) for h in range(2)]
        WK = [sb(f"WK{h}", [P, KT, 2, P], F16) for h in range(2)]
        WV = [sb(f"WV{h}", [P, KT, KV * HD], F16) for h in range(2)]
        WO = [sb(f"WO{h}", [P, KT, HID], F16) for h in range(2)]
        XT = [sb(f"XT{h}", [P, 3, KT, GROUP], F16) for h in range(2)]
        CT = sb("CT", [3 * EXPERTS, 2, GROUP], F16)
        SEL = sb("SEL", [3 * EXPERTS, CHUNKS, P], F16)
        ident = sb("ident", [P, P], F16)
        identf = sb("identf", [P, P])
        XN = sb("XN", [P, GT, HID])
        XS = [sb(f"XS{h}", [P, GT, HID], F16) for h in range(2)]
        stats = sb("stats", [P, GT, 6])
        mv = sb("mv", [P, GT, 2])
        var = sb("var", [P, GT])
        rs = sb("rs", [P, GT])
        nw = sb("nw", [P, GT])
        rstd = sb("rstd", [P, GT])
        mhalf = sb("mhalf", [P, GT])
        pad = sb("pad", [P, 1])
        lmax = sb("lmax", [P, GT])
        ld = sb("ld", [P, GT, EXPERTS])
        pr = sb("pr", [P, GT, EXPERTS + TOPK])
        prz = sb("prz", [P, GT, EXPERTS + TOPK])
        r1 = sb("r1", [P, GT])
        top = sb("top", [P, GT, TOPK])
        ren = sb("ren", [P, GT, TOPK])
        cum = sb("cum", [P, GT, TOPK])
        carry = sb("carry", [P, GT, TOPK])
        keep = sb("keep", [P, GT, TOPK])
        rw = sb("rw", [P, GT, TOPK])
        comb = sb("comb", [P, GT, EXPERTS])
        cparts = sb("cparts", [P, GT, 3, EXPERTS], F16)
        amax = sb("amax", [P, N_SCALES])
        wmax = sb("wmax", [P, N_SCALES])
        rmax = sb("rmax", [P, N_SCALES])
        up = sb("up", [P, N_SCALES])
        fac = sb("fac", [P, 8])
        F_SILU, F_H, F_Y, F_LOGIT, F_EXP, F_O, F_T = (fac[:, i:i + 1] for i in range(7))

        ARENA = 14900
        arena = sb("arena", [P, ARENA])

        def carve(sizes):
            at, views = 0, []
            for n, dt in sizes:
                words = n if dt == F32 else n // 2
                v = arena[:, at:at + words]
                views.append(v if dt == F32 else v.bitcast(dt))
                at += words
            assert at <= ARENA, at
            return views

        n_gu, n_d = KT * 2 * CHUNKS * P, CHUNKS * HID
        n_small = [KT * EXPERTS, KT * KV * P, KT * 2 * P, KT * KV * HD, KT * HID]
        st_gu, st_g, st_q, st_k, st_v, st_o = carve([(n, F32) for n in [n_gu] + n_small])
        (st_d,) = carve([(n_d, F32)])
        s_f, t_f, w_f, h_hi_f, h_lo_f, qtab, kcos, ksin, ra, rb, rc, qo_hi, qo_lo, vb_f = carve(
            [(2 * GROUP, F32), (GROUP, F32), (GROUP, F32), (2 * GROUP, F16), (2 * GROUP, F16)]
            + [(SEQ, F32)] * 3 + [(GROUP, F32)] * 3 + [(5 * GROUP, F16)] * 2 + [(GT * KV * 32, F32)])
        silu = s_f.rearrange("p (b n) -> p b n", b=2)
        hs = [v.rearrange("p (b n) -> p b n", b=2) for v in (h_hi_f, h_lo_f)]
        qo = [v.rearrange("p (j n) -> p j n", j=5) for v in (qo_hi, qo_lo)]
        vb = vb_f.rearrange("p (t j c) -> p t j c", t=GT, j=KV)
        (qst_f, kst_f, vst_f, pe_f, oT, otok_f, oh_f, ol_f, th_f, tl_f, mx2_f, mx_f, ml_f, rd_f, mT) = carve(
            [(2 * REP * SEQ, F16), (2 * SEQ, F16), (2 * QT * 32, F32), (NP_BUF * SEQ, F32), (SEQ, F32),
             (QT * P, F32), (QT * P, F16), (QT * P, F16), (SEQ, F16), (SEQ, F16), (QT * REP * 2, F32),
             (QT * REP, F32), (QT * 2 * REP, F16), (QT * REP, F32), (SEQ, F16)])
        qst = qst_f.rearrange("p (s i n) -> p s i n", s=2, i=REP)
        kst = kst_f.rearrange("p (s n) -> p s n", s=2)
        vst = vst_f.rearrange("p (s t c) -> p s t c", s=2, t=QT)
        pex = pe_f.rearrange("p (b n) -> p b n", b=NP_BUF)
        otok = otok_f.rearrange("p (t u c) -> p t u c", t=QT, u=2)
        osp = [oh_f, ol_f]
        oTT = [th_f, tl_f]
        mx2 = mx2_f.rearrange("p (t i h) -> p t i h", t=QT, i=REP)
        mx = mx_f.rearrange("p (t i) -> p t i", t=QT)
        ml = ml_f.rearrange("p (t a i) -> p t a i", t=QT, a=2)
        rd = rd_f.rearrange("p (t i) -> p t i", t=QT)

        q_d = nc.dram_tensor("q_scratch", (2, BATCH, KV, P, SEQ), F16, kind="Internal").ap()
        k_d = nc.dram_tensor("k_scratch", (2, BATCH, P, SEQ), F16, kind="Internal").ap()
        v_d = nc.dram_tensor("v_scratch", (BATCH, KV, P, QT, 32), F32, kind="Internal").ap()

        PS = ctx.enter_context(nc.psum_tensor("PS", [P, 8, 512], F32))

        def bank16(b):
            return PS[:, b, :].bitcast(F16)

        gu_in, small_in, x_in, d_in = sem("gu_in"), sem("small_in"), sem("x_in"), sem("d_in")
        const_in, tab_in, consts_set = sem("const_in"), sem("tab_in"), sem("consts_set")
        amax_gu, amax_all, wmax_all = sem("amax_gu"), sem("amax_all"), sem("wmax_all")
        amax_d, wmax_d = sem("amax_d"), sem("wmax_d")
        scales_set, gu_split, d_split, small_split = sem("scales_set"), sem("gu_split"), sem("d_split"), sem("small_split")
        setup_link = sem("setup_link")

        class LayerSignals:

            def __init__(self, n):
                self.g_done = sem(f"g_done_{n}")
                self.u_done = sem(f"u_done_{n}")
                self.c_done = sem(f"c_done_{n}")
                self.silu_done = sem(f"silu_done_{n}")
                self.gated = sem(f"gated_{n}")
                self.weighted = sem(f"weighted_{n}")
                self.hi_done = sem(f"hi_done_{n}")
                self.split = sem(f"split_{n}")
                self.y_done = sem(f"y_done_{n}")
                self.x_done = sem(f"x_done_{n}")

        class NormSignals:

            def __init__(self, n):
                self.norm_link = sem(f"norm_link_{n}")
                self.var_ready = sem(f"var_ready_{n}")
                self.rs_ready = sem(f"rs_ready_{n}")
                self.xs_ready = sem(f"xs_ready_{n}")
                self.t_hi = sem(f"t_hi_{n}")
                self.t_lo = sem(f"t_lo_{n}")
                self.xt_hi = sem(f"xt_hi_{n}")
                self.xt_lo = sem(f"xt_lo_{n}")

        class RouteSignals:

            def __init__(self, n):
                self.route_link = sem(f"route_link_{n}")
                self.logits = sem(f"logits_{n}")
                self.diff_ready = sem(f"diff_ready_{n}")
                self.exp_ready = sem(f"exp_ready_{n}")
                self.parts_ready = sem(f"parts_ready_{n}")
                self.ct_done = sem(f"ct_done_{n}")
                self.ct_ready = sem(f"ct_ready_{n}")

        L = [LayerSignals(n) for n in range(2)]
        N = [NormSignals(n) for n in range(3)]
        R = [RouteSignals(n) for n in range(2)]
        j_done = sem("j_done")
        rope_link, qo_ready, vb_ready, qo_out, vb_out, vb_set = (
            sem("rope_link"), sem("qo_ready"), sem("vb_ready"), sem("qo_out"), sem("vb_out"), sem("vb_set"))
        q_in, v_in, rows_in = ([sem(f"{k}{w}") for w in range(2)] for k in ("q_in", "v_in", "rows_in"))
        const_rows = sem("const_rows")
        max_ready, max_taken = sem("max_ready"), sem("max_taken")
        exp_in, exp_done, pv_done = sem("exp_in"), sem("exp_done"), sem("pv_done")
        rows_link, rows_split, rows_T, rows_sb = (
            sem("rows_link"), sem("rows_split"), sem("rows_T"), sem("rows_sb"))
        o_sb, o_T, o_link, o_norm, o_split, oT_done, oT_sb, yo_done, xo_done = (
            sem("o_sb"), sem("o_T"), sem("o_link"), sem("o_norm"), sem("o_split"), sem("oT_done"), sem("oT_sb"),
            sem("yo_done"), sem("xo_done"))
        stored = sem("stored")

        block = ctx.enter_context(nc.Block())

        PASSES = ((0, 0), (0, 1), (1, 0))

        class Link:

            def __init__(self, eng, s, per):
                self.eng, self.s, self.per, self.n, self.turn = eng, s, per, 0, 0

            def start(self, turn):
                self.turn, self.n = turn, 0

            def __call__(self, ins):
                self.n += 1
                ins.then_inc(self.s, 1)
                self.eng.wait_ge(self.s, self.turn * self.per + self.n)

            def many(self, instructions):
                for ins in instructions:
                    self.n += 1
                    ins.then_inc(self.s, 1)
                self.eng.wait_ge(self.s, self.turn * self.per + self.n)

            def end(self):
                assert self.n == self.per, (self.n, self.per)

        @block.sync
        def _(sp):
            for k in range(KT):
                n = n_gu // KT
                sp.dma_start(st_gu[:, k * n:(k + 1) * n], wgu[:, k * n:(k + 1) * n]).then_inc(gu_in, 16)
            sp.dma_start(X[:, :, :], x.rearrange("(i p) h -> p i h", p=P)).then_inc(x_in, 16)
            sp.wait_ge(gu_split, 1)
            sp.wait_ge(small_split, 1)
            sp.dma_start(st_d, wd).then_inc(d_in, 16)

            sp.wait_ge(d_split, 1)
            for t, v in enumerate((qtab, kcos, ksin)):
                sp.dma_start(v, (qtab_c if t == 0 else ktab_c[t - 1])).then_inc(tab_in, 16)
            with sp.Fori(0, BATCH) as b:
                for hf in range(2):
                    g = b * 2 + hf
                    cols = slice(hf * GROUP, (hf + 1) * GROUP)
                    sp.wait_ge(x_in, 16)
                    sp.wait_ge(qo_ready, g + 1)
                    for h in range(2):
                        sp.dma_start(q_d[h, bass.ds(b, 1), :, :, cols].rearrange("a j p n -> p (a j) n"),
                                     qo[h][:, 0:KV, :]).then_inc(qo_out, 16)
                        sp.dma_start(k_d[h, bass.ds(b, 1), :, cols].rearrange("a p n -> p (a n)"),
                                     qo[h][:, KV, :]).then_inc(qo_out, 16)
                    sp.wait_ge(x_in, 16)
                    sp.wait_ge(vb_ready, g + 1)
                    for j in range(KV):
                        sp.dma_start(v_d[bass.ds(b, 1), j, :, hf * GT:(hf + 1) * GT, :]
                                     .rearrange("a p t c -> p (a t) c"), vb[:, :, j, :]).then_inc(vb_out, 16)

            sp.wait_ge(qo_out, 64 * GROUPS)
            sp.wait_ge(vb_out, 64 * GROUPS)

            def load(b, j, u, slot, first):
                if not first:
                    sp.wait_ge(x_in, 16)
                    sp.wait_ge(exp_in, (u - 1) * 32)
                for r, h in enumerate((0, 0, 1)):
                    sp.dma_start(qst[32 * r:32 * r + 32, slot, :, :],
                                 q_d[h, bass.ds(b, 1), j, :, :].rearrange("a (i r) n -> r (a i) n", i=REP))\
                      .then_inc(q_in[slot], 16)
                for r, h in enumerate((0, 1, 0)):
                    sp.dma_start(kst[32 * r:32 * r + 32, slot, :],
                                 k_d[h, bass.ds(b, 1), 32 * j:32 * j + 32, :].rearrange("a r n -> r (a n)"))\
                      .then_inc(q_in[slot], 16)
                if not first:
                    sp.wait_ge(x_in, 16)
                    sp.wait_ge(pv_done, (u - 1) * 32)
                sp.dma_start(vst[:, slot, :, :],
                             v_d[bass.ds(b, 1), j, :, :, :].rearrange("a p t c -> p (a t) c")).then_inc(v_in[slot], 16)

            def rows(u, slot):
                sp.wait_ge(rows_sb, u + 1)
                for a in range(2):
                    for i in range(REP):
                        sp.dma_start(qst[96 + a:97 + a, slot, i, :], mT[a * REP + i:a * REP + i + 1, :])\
                          .then_inc(rows_in[slot], 16)

            for w in range(2):
                load(0, w, w, w, True)
            rows(0, 0)
            rows(1, 1)
            load(0, 2, 2, 0, False)
            rows(2, 0)
            load(0, 3, 3, 1, False)
            rows(3, 1)
            with sp.Fori(1, BATCH) as b:
                for j in range(KV):
                    load(b, j, b * KV + j, j % 2, False)
                    rows(b * KV + j, j % 2)

            with sp.Fori(0, GROUPS) as g:
                sp.wait_ge(x_in, 16)
                sp.wait_ge(L[1].x_done, g + 2)
                sp.dma_start(out.rearrange("(i p) h -> p i h", p=P)[:, bass.ds(g * GT, GT), :],
                             X[:, bass.ds(g * GT, GT), :]).then_inc(stored, 16)
            sp.wait_ge(stored, 16 * GROUPS)
        @block.gpsimd
        def _(pool):
            pool.memset(mhalf[:, :], -0.5).then_inc(consts_set, 1)
            pool.wait_ge(consts_set, 1)
            pool.wait_ge(amax_all, 1)
            pool.partition_all_reduce(wmax[:, :], amax[:, :], P, ABSMAX).then_inc(wmax_all, 1)
            pool.wait_ge(amax_d, 1)
            pool.partition_all_reduce(wmax[:, S_D:S_D + 1], amax[:, S_D:S_D + 1], P, ABSMAX).then_inc(wmax_d, 1)

            def inverse_roots(n, k):
                pool.wait_ge(n.var_ready, k + 1)
                pool.tensor_tensor(rs[:, :], var[:, :], mhalf[:, :], ALU.pow).then_inc(n.rs_ready, 1)

            def layer(n, proj):
                inverse_roots(n, 0)
                inverse_roots(n, 1)
                with pool.Fori(1, GROUPS) as g:
                    inverse_roots(n, g + 1)
                    if proj:
                        inverse_roots(proj, g - 1)
                if proj:
                    inverse_roots(proj, GROUPS - 1)

            layer(N[0], N[1])
            layer(N[2], None)

        @block.scalar
        def _(act):
            for v, src in ((st_g, wg), (st_q, wq), (st_k, wk), (st_v, wv), (st_o, wo)):
                act.dma_start(v, src).then_inc(small_in, 16)
            act.dma_start(SEL[:, :, :], sel_c).then_inc(const_in, 16)
            act.dma_start(ident[:, :], ident_c).then_inc(const_in, 16)

            def take_rows(n, k, slot, h):
                act.wait_ge((n.t_hi, n.t_lo)[h], k + 1)
                act.activation(XT[h][:, slot, :, :].rearrange("p a k n -> p (a k n)"), bank16(B_PREP), ACT.Copy)\
                   .then_inc((n.xt_hi, n.xt_lo)[h], 1)

            def exponentials(r, k):
                act.wait_ge(r.diff_ready, k + 1)
                act.activation(pr[:, :, 0:EXPERTS], ld[:, :, :], ACT.Exp, scale=F_LOGIT).then_inc(r.exp_ready, 1)

            def take_combine(r, k, slot):
                act.wait_ge(r.ct_done, k + 1)
                act.activation(CT[:, slot, :].rearrange("p a n -> p (a n)"), bank16(B_PREP)[0:3 * EXPERTS, 0:GROUP],
                               ACT.Copy).then_inc(r.ct_ready, 1)

            def layer(lay, n, r, proj):
                def gate(m, c):
                    act.wait_ge(lay.g_done, m + 1)
                    act.activation(silu[:, c % 2, :], PS[:, B_G + c % 2, :], ACT.Silu, scale=F_SILU)\
                       .then_inc(lay.silu_done, 1)

                def group(g, first):
                    nxt = bass.ds((g + 1) % 2, 1)
                    for s in range(CHUNKS):
                        gate(g * CHUNKS + s + 1, s + 1)
                        if s == N0_T_HI + 1:
                            take_rows(n, g + 1, nxt, 0)
                        if s == N0_T_LO + 1:
                            take_rows(n, g + 1, nxt, 1)
                        if s == R_EXP:
                            exponentials(r, g + 1)
                        if s == R_T + 1:
                            take_combine(r, g + 1, nxt)
                        if proj and not first:
                            if s == N1_T_HI + 1:
                                take_rows(proj, g - 1, bass.ds(2, 1), 0)
                            if s == N1_T_LO + 1:
                                take_rows(proj, g - 1, bass.ds(2, 1), 1)

                take_rows(n, 0, bass.ds(0, 1), 0)
                take_rows(n, 0, bass.ds(0, 1), 1)
                exponentials(r, 0)
                take_combine(r, 0, bass.ds(0, 1))
                gate(0, 0)
                group(0, True)
                with act.Fori(1, GROUPS) as g:
                    group(g, False)
                if proj:
                    for h in range(2):
                        take_rows(proj, GROUPS - 1, bass.ds(2, 1), h)

            act.wait_ge(scales_set, 1)
            layer(L[0], N[0], R[0], N[1])

            def exps(T, t):
                act.wait_ge(exp_in, T + 1)
                if not (isinstance(T, int) and T < NP_BUF):
                    act.wait_ge(pv_done, T - NP_BUF + 1)
                b = B_EXP + 2 * (t % 2)
                act.activation(pex[:, t % NP_BUF, :], PS[:, b:b + 2, :].rearrange("p a n -> p (a n)"), ACT.Exp,
                               scale=F_EXP).then_inc(exp_done, 1)

            def take_outputs(u):
                act.wait_ge(pv_done, (u + 1) * 32)
                if not (isinstance(u, int) and u == 0):
                    act.wait_ge(o_T, u)
                act.activation(oT, PS[:, B_OUT:B_OUT + 2, :].rearrange("p a n -> p (a n)"), ACT.Copy)\
                   .then_inc(o_sb, 1)

            def take_max_rows(u, v, w):
                act.wait_ge(rows_T, u + 1)
                if w == 1:
                    act.wait_ge(rows_in[0], 128 * (v + 1))
                elif not (isinstance(u, int) and u == 0):
                    act.wait_ge(rows_in[1], 128 * v)
                act.activation(mT[0:2 * REP, :], bank16(B_MAX)[0:2 * REP, :], ACT.Copy).then_inc(rows_sb, 1)

            def take_otok(v):
                for h in range(2):
                    act.wait_ge(oT_done, 2 * v + h + 1)
                    act.activation(oTT[h], bank16(B_MAX + h), ACT.Copy).then_inc(oT_sb, 1)

            def pair(v, first, last):
                for w in range(2):
                    u = 2 * v + w
                    for t in range(32):
                        if t == LAG and not (first and w == 0):
                            take_outputs(u - 1)
                        exps(u * 32 + t, w * 32 + t)
                        if t == 1 and w == 1 and not first:
                            take_otok(v - 1)
                        if t == MAX_TO and not (last and w == 1):
                            take_max_rows(u + 1, v + w, 1 - w)

            take_max_rows(0, 0, 0)
            pair(0, True, False)
            with act.Fori(1, UNITS // 2 - 1) as v:
                pair(v, False, False)
            pair(UNITS // 2 - 1, False, True)
            take_outputs(UNITS - 1)
            take_otok(UNITS // 2 - 1)

            layer(L[1], N[2], R[1], None)

        @block.vector
        def _(dve):
            dve.memset(pr[:, :, EXPERTS:], 2.0).then_inc(consts_set, 1)
            dve.memset(carry[:, :, :], 1.0).then_inc(consts_set, 1)
            dve.memset(amax[:, :], 0.0).then_inc(consts_set, 1)
            dve.wait_ge(consts_set, 4)
            dve.memset(carry[:, :, 0:1], 0.0).then_inc(consts_set, 1)
            dve.memset(keep[:, :, 0:1], 1.0).then_inc(consts_set, 1)
            dve.wait_ge(const_in, 32)
            dve.tensor_copy(identf[:, :], ident[:, :]).then_inc(consts_set, 1)
            dve.wait_ge(consts_set, 7)

            link = Link(dve, setup_link, 10 ** 6)

            small = ((S_G, st_g), (S_Q, st_q), (S_K, st_k), (S_V, st_v), (S_O, st_o))
            dve.wait_ge(small_in, 16 * len(small))
            for s, v in small:
                link(dve.tensor_reduce(amax[:, s:s + 1], v, AX_X, ALU.max, apply_absolute_value=True))
            dve.wait_ge(gu_in, 32)
            dve.tensor_reduce(amax[:, S_GU:S_GU + 1], st_gu, AX_X, ALU.max, apply_absolute_value=True)\
               .then_inc(amax_all, 1)

            def power_of_two(a, b):
                link(dve.tensor_scalar(wmax[:, a:b], wmax[:, a:b], 2.0 ** -60, None, ALU.max))
                link(dve.tensor_scalar(wmax[:, a:b].bitcast(I32), wmax[:, a:b].bitcast(I32), 0x7F800000, None,
                                       ALU.bitwise_and))
                link(dve.reciprocal(rmax[:, a:b], wmax[:, a:b]))
                link(dve.tensor_scalar(up[:, a:b], rmax[:, a:b], W_UP, None, ALU.mult))

            def split_weights(s, v, hi, lo):
                link(dve.tensor_scalar(hi, v, up[:, s:s + 1], None, ALU.mult))
                return dve.scalar_tensor_tensor(lo, v, up[:, s:s + 1], hi, ALU.mult, ALU.subtract)

            def flat(t):
                return t.rearrange("p a b -> p (a b)") if len(t.shape) == 3 else t.rearrange("p a b c -> p (a b c)")

            dve.wait_ge(wmax_all, 1)
            power_of_two(0, N_SCALES)
            mul = ALU.mult
            link(dve.tensor_scalar(F_SILU, wmax[:, S_GU:S_GU + 1], 1 / XW, None, mul))
            link(dve.tensor_scalar(F_LOGIT, wmax[:, S_G:S_G + 1], 1 / XW, None, mul))
            link(dve.tensor_scalar(F_H, rmax[:, S_GU:S_GU + 1], 2.0 ** -35, None, mul))
            link(dve.scalar_tensor_tensor(F_EXP, wmax[:, S_Q:S_Q + 1], HD ** -0.5 / 64, wmax[:, S_K:S_K + 1],
                                          mul, mul))
            link(dve.scalar_tensor_tensor(F_O, wmax[:, S_V:S_V + 1], 2.0 ** -18, wmax[:, S_O:S_O + 1], mul, mul))
            link(split_weights(S_G, st_g, flat(WG[0]), flat(WG[1])))
            link(split_weights(S_Q, st_q, flat(WQ[0]), flat(WQ[1])))
            link(split_weights(S_K, st_k, flat(WK[0]), flat(WK[1])))
            link(split_weights(S_V, st_v, flat(WV[0]), flat(WV[1])))
            split_weights(S_O, st_o, flat(WO[0]), flat(WO[1])).then_inc(small_split, 1)
            split_weights(S_GU, st_gu, flat(WGU[0]), flat(WGU[1])).then_inc(gu_split, 1)
            dve.wait_ge(small_split, 1)
            dve.wait_ge(gu_split, 1)
            dve.wait_ge(d_in, 16)
            dve.tensor_reduce(amax[:, S_D:S_D + 1], st_d, AX_X, ALU.max, apply_absolute_value=True)\
               .then_inc(amax_d, 1)
            dve.wait_ge(wmax_d, 1)
            power_of_two(S_D, S_D + 1)
            link(dve.scalar_tensor_tensor(F_T, wmax[:, S_GU:S_GU + 1], 2.0 ** -10, wmax[:, S_GU:S_GU + 1], mul, mul))
            dve.tensor_scalar(F_Y, F_T, wmax[:, S_D:S_D + 1], None, mul).then_inc(scales_set, 1)
            split_weights(S_D, st_d, flat(WD[0]), flat(WD[1])).then_inc(d_split, 1)
            dve.wait_ge(scales_set, 1)
            dve.wait_ge(d_split, 1)

            def carry_wait():
                return dve.memset(pad[:, :], 0.0)

            def norm(n, lk, k, G, piece, reads=None):
                def rows(i):
                    return X[:, bass.ds(G * GT + i, 1), :].rearrange("p a h -> p (a h)")

                def normed(i):
                    return dve.tensor_scalar(XN[:, i, :], rows(i), mv[:, i, 0:1], rstd[:, i:i + 1],
                                             ALU.subtract, ALU.mult)

                if piece == 0:
                    lk.start(k)
                    lk.many(dve.bn_stats(stats[:, i, :], rows(i)) for i in range(3))
                if piece == 1:
                    lk.many(dve.bn_stats(stats[:, i, :], rows(i)) for i in range(3, GT))
                    carry_wait()
                    lk.many(dve.bn_aggr(mv[:, i, :], stats[:, i, :]) for i in range(GT))
                    dve.tensor_scalar(var[:, :], mv[:, :, 1], EPS, None, ALU.add).then_inc(n.var_ready, 1)
                if piece == 2:
                    dve.wait_ge(n.rs_ready, k + 1)
                    lk(dve.tensor_tensor(nw[:, :], rs[:, :], rs[:, :], ALU.mult))
                    lk(dve.tensor_tensor(nw[:, :], nw[:, :], var[:, :], ALU.mult))
                    lk(dve.tensor_scalar(nw[:, :], nw[:, :], -0.5 * X_UP, 1.5 * X_UP, ALU.mult, ALU.add))
                    lk(dve.tensor_tensor(rstd[:, :], nw[:, :], rs[:, :], ALU.mult))
                    lk.many(normed(i) for i in range(2))
                if piece == 3:
                    lk.many(normed(i) for i in range(2, GT))
                    if reads:
                        dve.wait_ge(*reads)
                    lk(dve.tensor_copy(flat(XS[0]), flat(XN)))
                if piece == 4:
                    dve.tensor_tensor(flat(XS[1]), flat(XN), flat(XS[0]), ALU.subtract).then_inc(n.xs_ready, 1)
                    lk.end()

            NORM_LINKS = GT + GT + 4 + GT + 1

            def route(r, lk, k, piece):
                LG = PS[:, B_PREP, 0:GT * EXPERTS].rearrange("p (t e) -> p t e", t=GT)
                PR = pr[:, :, 0:EXPERTS]
                if piece == 0:
                    dve.wait_ge(r.logits, k + 1)
                    lk.start(k)
                    lk(dve.tensor_reduce(lmax[:, :], LG, AX_X, ALU.max))
                    dve.tensor_tensor(ld[:, :, :], LG, lmax[:, :].unsqueeze(2).to_broadcast([P, GT, EXPERTS]),
                                      ALU.subtract).then_inc(r.diff_ready, 1)
                if piece == 1:
                    dve.wait_ge(r.exp_ready, k + 1)
                    lk(dve.tensor_reduce(r1[:, :], PR, AX_X, ALU.add))
                    lk(dve.reciprocal(r1[:, :], r1[:, :]))
                    lk(dve.tensor_tensor(PR, PR, r1[:, :].unsqueeze(2).to_broadcast([P, GT, EXPERTS]), ALU.mult))
                    carry_wait()
                    lk.many(dve.max(top[:, i, :], pr[:, i, 0:EXPERTS]) for i in range(GT))
                if piece == 2:
                    lk(dve.tensor_reduce(r1[:, :], top[:, :, :], AX_X, ALU.add))
                    lk(dve.tensor_scalar(r1[:, :], r1[:, :], 1e-12, None, ALU.max))
                    lk(dve.reciprocal(r1[:, :], r1[:, :]))
                    lk(dve.tensor_tensor(ren[:, :, :], top[:, :, :],
                                         r1[:, :].unsqueeze(2).to_broadcast([P, GT, TOPK]), ALU.mult))
                if piece == 3:
                    lk(dve.tensor_tensor_scan(flat(cum), flat(carry), flat(ren), 0.0, ALU.mult, ALU.add))
                    lk(dve.tensor_scalar(keep[:, :, 1:TOPK], cum[:, :, 0:TOPK - 1], KEEP_BELOW, None, ALU.is_lt))
                    lk(dve.tensor_tensor(rw[:, :, :], top[:, :, :], keep[:, :, :], ALU.mult))
                    lk(dve.tensor_reduce(r1[:, :], rw[:, :, :], AX_X, ALU.add))
                if piece == 4:
                    lk(dve.tensor_scalar(r1[:, :], r1[:, :], 1e-12, None, ALU.max))
                    lk(dve.reciprocal(r1[:, :], r1[:, :]))
                    lk(dve.tensor_scalar(ren[:, :, :], keep[:, :, :], -2.0, 2.0, ALU.mult, ALU.add))
                    lk(dve.tensor_tensor(rw[:, :, :], rw[:, :, :], ren[:, :, :], ALU.add))
                if piece == 5:
                    carry_wait()
                    lk.many(dve.match_replace(prz[:, i, :], rw[:, i, :], pr[:, i, :], 0.0) for i in range(GT))
                    lk(dve.tensor_tensor(comb[:, :, :], PR, prz[:, :, 0:EXPERTS], ALU.subtract))
                if piece == 6:
                    lk(dve.tensor_scalar(r1[:, :], r1[:, :], C_UP, None, ALU.mult))
                    lk(dve.tensor_tensor(comb[:, :, :], comb[:, :, :],
                                         r1[:, :].unsqueeze(2).to_broadcast([P, GT, EXPERTS]), ALU.mult))
                    lk(dve.tensor_copy(cparts[:, :, 0, :], comb[:, :, :]))
                    lk(dve.tensor_tensor(comb[:, :, :], comb[:, :, :], cparts[:, :, 0, :], ALU.subtract))
                if piece == 7:
                    lk(dve.tensor_copy(cparts[:, :, 1, :], comb[:, :, :]))
                    dve.tensor_tensor(cparts[:, :, 2, :], comb[:, :, :], cparts[:, :, 1, :], ALU.subtract)\
                       .then_inc(r.parts_ready, 1)
                    lk.end()

            ROUTE_LINKS = 1 + 7 + 4 + 4 + 4 + 5 + 4 + 1

            HALF = 2.0 ** 3 / XW

            def project(jl, k, cols, piece, first):
                dve.wait_ge(j_done, k * 7 + piece + 1)
                J = PS[:, B_PREP, :]
                if piece == 0:
                    jl.start(k)
                    if not first:
                        dve.wait_ge(qo_out, k * 64)
                if piece < KV:
                    r = (ra, rb)[piece % 2]
                    jl(dve.scalar_tensor_tensor(r, J, HALF, qtab[:, cols], ALU.mult, ALU.mult))
                    jl(dve.tensor_copy(qo[0][:, piece, :], r))
                    jl(dve.tensor_tensor(qo[1][:, piece, :], r, qo[0][:, piece, :], ALU.subtract))
                if piece == KV:
                    jl(dve.scalar_tensor_tensor(ra, J, HALF, kcos[:, cols], ALU.mult, ALU.mult))
                if piece == KV + 1:
                    jl(dve.scalar_tensor_tensor(rb, J, HALF, ksin[:, cols], ALU.mult, ALU.mult))
                    jl(dve.tensor_tensor(rc, ra, rb, ALU.add))
                    jl(dve.tensor_copy(qo[0][:, KV, :], rc))
                    dve.tensor_tensor(qo[1][:, KV, :], rc, qo[0][:, KV, :], ALU.subtract).then_inc(qo_ready, 1)
                    jl.end()
                if piece == KV + 2:
                    if not first:
                        dve.wait_ge(vb_out, k * 64)
                    dve.tensor_scalar(vb[:, :, :, 0:HD],
                                      J[:, 0:GT * KV * HD].rearrange("p (t j d) -> p t j d", t=GT, j=KV),
                                      2.0 ** 6 / XW, None, ALU.mult).then_inc(vb_ready, 1)

            def layer(lay, n, r, proj):
                nl, rl = Link(dve, n.norm_link, NORM_LINKS), Link(dve, r.route_link, ROUTE_LINKS)
                if proj:
                    pl, jl = Link(dve, proj.norm_link, NORM_LINKS), Link(dve, rope_link, ROPE_LINKS)

                def weigh(m, c):
                    dve.wait_ge(lay.silu_done, m + 1)
                    dve.wait_ge(lay.u_done, m + 1)
                    dve.tensor_tensor(t_f, silu[:, c % 2, :], PS[:, B_U + c % 2, :], ALU.mult)\
                       .then_inc(lay.gated, 1)
                    dve.wait_ge(lay.gated, m + 1)
                    dve.wait_ge(lay.c_done, m + 1)
                    dve.scalar_tensor_tensor(w_f, t_f, F_H, PS[:, B_C, :], ALU.mult, ALU.mult)\
                       .then_inc(lay.weighted, 1)
                    dve.wait_ge(lay.weighted, m + 1)
                    dve.tensor_copy(hs[0][:, c % 2, :], w_f).then_inc(lay.hi_done, 1)
                    dve.wait_ge(lay.hi_done, m + 1)
                    dve.tensor_tensor(hs[1][:, c % 2, :], w_f, hs[0][:, c % 2, :], ALU.subtract)\
                       .then_inc(lay.split, 1)

                def group(g, first):
                    nxt = (g + 1) % GROUPS
                    for s in range(CHUNKS):
                        weigh(g * CHUNKS + s + 1, s + 1)
                        if s in N0_DVE:
                            norm(n, nl, g + 1, nxt, N0_DVE.index(s))
                        if s in R_DVE:
                            route(r, rl, g + 1, R_DVE.index(s))
                        if proj and not first:
                            cols = bass.ds((g - 1) % 2 * GROUP, GROUP)
                            if s in N1_DVE:
                                norm(proj, pl, g - 1, g - 1, N1_DVE.index(s), (n.t_lo, g + 2))
                            if s in J_AT:
                                project(jl, g - 1, cols, J_AT.index(s), isinstance(g, int))
                    dve.wait_ge(lay.y_done, g + 1)
                    for b in range(2):
                        xv = X[:, bass.ds(g * GT + 2 * b, 2), :].rearrange("p a h -> p (a h)")
                        ins = dve.scalar_tensor_tensor(xv, PS[:, B_Y + b, :], F_Y, xv, ALU.mult, ALU.add)
                    ins.then_inc(lay.x_done, 1)
                    dve.wait_ge(lay.x_done, g + 2)

                for piece in range(5):
                    norm(n, nl, 0, 0, piece)
                for piece in range(8):
                    route(r, rl, 0, piece)
                carry_wait().then_inc(lay.x_done, 1)
                weigh(0, 0)
                group(0, True)
                if proj:
                    group(1, False)
                with dve.Fori(2 if proj else 1, GROUPS) as g:
                    group(g, False)
                if proj:
                    for piece in range(5):
                        norm(proj, pl, GROUPS - 1, GROUPS - 1, piece)
                    for piece in range(7):
                        project(jl, GROUPS - 1, slice(GROUP, SEQ), piece, False)

            dve.wait_ge(tab_in, 48)
            dve.memset(vb_f, 0.0).then_inc(vb_set, 1)
            dve.wait_ge(vb_set, 1)
            dve.memset(vb[:, :, :, HD:HD + 1], 1.0).then_inc(vb_set, 1)
            dve.wait_ge(vb_set, 2)
            dve.wait_ge(x_in, 16)
            layer(L[0], N[0], R[0], N[1])

            dve.wait_ge(qo_out, 64 * GROUPS)
            dve.wait_ge(vb_out, 64 * GROUPS)
            dve.memset(kst[96:98, :, :], -M_UNIT).then_inc(const_rows, 1)
            ml_link = Link(dve, rows_link, 2)
            ol = Link(dve, o_link, 1)

            def maxima(u, parts):
                for part in parts:
                    t, hf = part // 2, part % 2
                    dve.wait_ge(max_ready, u * 64 + part + 1)
                    dve.tensor_reduce(mx2[:, t // REP, t % REP, hf:hf + 1], PS[:, B_MAX + hf, :], AX_X,
                                      ALU.max).then_inc(max_taken, 1)

            def max_rows(u):
                ml_link.start(u)
                dve.wait_ge(max_taken, (u + 1) * 64)
                ml_link(dve.tensor_reduce(mx, mx2, AX_X, ALU.max))
                ml_link(dve.tensor_scalar(ml[:, :, 0, :], mx, 1 / M_UNIT, None, ALU.mult))
                dve.scalar_tensor_tensor(ml[:, :, 1, :], mx, 1 / M_UNIT, ml[:, :, 0, :], ALU.mult,
                                         ALU.subtract).then_inc(rows_split, 1)

            def normalise(u, w):
                dve.wait_ge(o_T, u + 1)
                O = PS[:, B_MAX:B_MAX + 2, :].rearrange("p a n -> p (a n)")\
                    .rearrange("p (t i c) -> p t i c", t=QT, i=REP)
                ol.start(u)
                ol(dve.reciprocal(rd, O[:, :, :, HD]))
                dve.tensor_tensor(otok[:, :, w, :].rearrange("p t (i c) -> p t i c", i=REP), O[:, :, :, 0:HD],
                                  rd.unsqueeze(3).to_broadcast([P, QT, REP, HD]), ALU.mult).then_inc(o_norm, 1)

            def split_outputs(v):
                dve.wait_ge(o_norm, 2 * v + 2)
                dve.tensor_copy(osp[0], otok_f).then_inc(o_split, 1)
                dve.wait_ge(o_split, 2 * v + 1)
                dve.tensor_tensor(osp[1], otok_f, osp[0], ALU.subtract).then_inc(o_split, 1)

            def add_outputs(v, b, rnd):
                dve.wait_ge(yo_done, 2 * v + rnd + 1)
                xv = X[:, bass.ds(b * QT + rnd * 4, 4), :].rearrange("p a h -> p (a h)")
                dve.scalar_tensor_tensor(xv, PS[:, B_MAX:B_MAX + 2, :].rearrange("p a n -> p (a n)"), F_O, xv,
                                         ALU.mult, ALU.add).then_inc(xo_done, 1)
                dve.wait_ge(xo_done, 2 * v + rnd + 1)

            def pair(v, first, last):
                for w in range(2):
                    u = 2 * v + w
                    for t in range(32):
                        if not (last and w == 1):
                            for quarter in range(4):
                                maxima(u + 1, max_parts(t, quarter))
                            if t == MAX_TO:
                                max_rows(u + 1)
                        if t == LAG and not (first and w == 0):
                            normalise(u - 1, 1 - w)
                            if w == 0:
                                split_outputs(v - 1)
                        if w == 1 and not first and t in (1, 2):
                            add_outputs(v - 1, (v - 1) // 2, t - 1)

            maxima(0, range(64))
            max_rows(0)
            pair(0, True, False)
            with dve.Fori(1, UNITS // 2 - 1) as v:
                pair(v, False, False)
            v = UNITS // 2 - 1
            pair(v, False, True)
            normalise(UNITS - 1, 1)
            split_outputs(v)
            for rnd in range(2):
                add_outputs(v, v // 2, rnd)

            layer(L[1], N[2], R[1], None)

        @block.tensor
        def _(pe):
            def transpose_rows(n, k, h):
                if h == 0:
                    pe.wait_ge(n.xs_ready, k + 1)
                else:
                    pe.wait_ge(n.xt_hi, k + 1)
                for kt in range(KT):
                    for i in range(GT):
                        ins = pe.transpose(bank16(B_PREP)[:, kt * GROUP + i * P:kt * GROUP + (i + 1) * P],
                                           XS[h][:, i, kt * P:(kt + 1) * P], ident[:, :])
                ins.then_inc((n.t_hi, n.t_lo)[h], 1)

            def xt(h, slot, kt, lo=0, hi=GROUP):
                return XT[h][:, slot, kt, lo:hi].rearrange("p a n -> p (a n)")

            def logits(n, r, k, slot):
                pe.wait_ge(n.xt_lo, k + 1)
                for i in range(GT):
                    for m, (a, b) in enumerate(PASSES):
                        for kt in range(KT):
                            ins = pe.matmul(PS[:, B_PREP, i * EXPERTS:(i + 1) * EXPERTS],
                                            xt(b, slot, kt, i * P, (i + 1) * P), WG[a][:, kt, :],
                                            start=(m == 0 and kt == 0), stop=(m == 2 and kt == KT - 1))
                ins.then_inc(r.logits, 1)

            def transpose_combine(r, k):
                pe.wait_ge(r.parts_ready, k + 1)
                for i in range(GT):
                    ins = pe.transpose(bank16(B_PREP)[0:3 * EXPERTS, i * P:(i + 1) * P],
                                       cparts[:, i, :, :].rearrange("p a e -> p (a e)"), ident[:, :])
                ins.then_inc(r.ct_done, 1)

            def gate_up(lay, c, slot):
                for part, bank, s in ((0, B_G, lay.g_done), (1, B_U, lay.u_done)):
                    for m, (a, b) in enumerate(PASSES):
                        for kt in range(KT):
                            ins = pe.matmul(PS[:, bank + c % 2, :], WGU[a][:, kt, part * CHUNKS + c, :],
                                            xt(b, slot, kt), start=(m == 0 and kt == 0),
                                            stop=(m == 2 and kt == KT - 1))
                    ins.then_inc(s, 1)

            def product(ps, weights, rows, rows_first=False):
                for m, (a, b) in enumerate(PASSES):
                    for kt in range(KT):
                        lhs, rhs = (rows(b, kt), weights(a, kt)) if rows_first else (weights(a, kt), rows(b, kt))
                        ins = pe.matmul(ps, lhs, rhs, start=(m == 0 and kt == 0), stop=(m == 2 and kt == KT - 1))
                return ins

            def project(proj, k, piece):
                slot = bass.ds(2, 1)
                if piece == 0:
                    pe.wait_ge(proj.xt_lo, k + 1)
                else:
                    pe.wait_ge(rope_link, k * ROPE_LINKS + (1, 4, 7, 10, 13, 14)[piece - 1])
                if piece < KV:
                    ins = product(PS[:, B_PREP, :], lambda a, kt: WQ[a][:, kt, piece, :],
                                  lambda b, kt: xt(b, slot, kt))
                elif piece < KV + 2:
                    ins = product(PS[:, B_PREP, :], lambda a, kt: WK[a][:, kt, piece - KV, :],
                                  lambda b, kt: xt(b, slot, kt))
                else:
                    for i in range(GT):
                        ins = product(PS[:, B_PREP, i * KV * HD:(i + 1) * KV * HD], lambda a, kt: WV[a][:, kt, :],
                                      lambda b, kt: xt(b, slot, kt, i * P, (i + 1) * P), True)
                ins.then_inc(j_done, 1)

            def layer(lay, n, r, proj):
                zero = bass.ds(0, 1)

                def combine(c, slot):
                    pe.matmul(PS[:, B_C, :], SEL[:, c, :], CT[:, slot, :].rearrange("p a n -> p (a n)"),
                              start=True, stop=True).then_inc(lay.c_done, 1)

                def down(c):
                    for i in range(GT):
                        for m, (b, a) in enumerate(PASSES):
                            ins = pe.matmul(PS[:, B_Y + i // 2, (i % 2) * HID:(i % 2 + 1) * HID],
                                            hs[a][:, c % 2, i * P:(i + 1) * P], WD[b][:, c, :],
                                            start=(c == 0 and m == 0 and i % 2 == 0),
                                            stop=(c == CHUNKS - 1 and m == 2), skip_group_check=True)
                    return ins

                def group(g, first):
                    cur, nxt = bass.ds(g % 2, 1), bass.ds((g + 1) % 2, 1)
                    for s in range(CHUNKS):
                        m = g * CHUNKS + s
                        c, slot = (s + 1, cur) if s + 1 < CHUNKS else (0, nxt)
                        gate_up(lay, c, slot)
                        if c == 0:
                            pe.wait_ge(r.ct_ready, g + 2)
                        pe.wait_ge(lay.weighted, m + 1)
                        combine(c, slot)
                        pe.wait_ge(lay.split, m + 1)
                        if s == 0:
                            pe.wait_ge(lay.x_done, g + 1)
                        ins = down(s)
                        if s == CHUNKS - 1:
                            ins.then_inc(lay.y_done, 1)
                        if s == N0_T_HI:
                            if proj and not first and not (isinstance(g, int) and g == 1):
                                pe.wait_ge(vb_ready, g - 1)
                            transpose_rows(n, g + 1, 0)
                        if s == N0_T_LO:
                            transpose_rows(n, g + 1, 1)
                        if s == LOGITS:
                            logits(n, r, g + 1, nxt)
                        if s == R_T:
                            if proj and not first:
                                pe.wait_ge(rope_link, (g - 1) * ROPE_LINKS + 10)
                            transpose_combine(r, g + 1)
                        if proj and not first:
                            if s == N1_T_HI:
                                pe.wait_ge(r.diff_ready, g + 2)
                                transpose_rows(proj, g - 1, 0)
                            if s == N1_T_LO:
                                transpose_rows(proj, g - 1, 1)
                            if s in J_AT:
                                if s == J_AT[KV]:
                                    pe.wait_ge(r.ct_ready, g + 2)
                                project(proj, g - 1, J_AT.index(s))

                transpose_rows(n, 0, 0)
                transpose_rows(n, 0, 1)
                logits(n, r, 0, zero)
                transpose_combine(r, 0)
                gate_up(lay, 0, zero)
                pe.wait_ge(r.ct_ready, 1)
                combine(0, zero)
                group(0, True)
                if proj:
                    group(1, False)
                with pe.Fori(2 if proj else 1, GROUPS) as g:
                    group(g, False)
                if proj:
                    pe.wait_ge(vb_ready, GROUPS - 1)
                    transpose_rows(proj, GROUPS - 1, 0)
                    transpose_rows(proj, GROUPS - 1, 1)
                    for piece in range(7):
                        project(proj, GROUPS - 1, piece)

            pe.wait_ge(consts_set, 7)
            pe.wait_ge(small_split, 1)
            pe.wait_ge(gu_split, 1)
            pe.wait_ge(d_split, 1)
            layer(L[0], N[0], R[0], N[1])

            def score_max(u, slot, parts, first=False):
                for part in parts:
                    t, hf = part // 2, part % 2
                    if not (first and part < 2):
                        pe.wait_ge(max_taken, u * 64 + part - 1)
                    pe.matmul(PS[:, B_MAX + hf, :],
                              qst[0:96, slot, t % REP, (t // REP) * P:(t // REP + 1) * P],
                              kst[0:96, slot, hf * 512:(hf + 1) * 512], start=True, stop=True)\
                      .then_inc(max_ready, 1)

            def transpose_max(u):
                pe.wait_ge(rows_split, u + 1)
                for t in range(QT):
                    ins = pe.transpose(bank16(B_MAX)[0:2 * REP, t * P:(t + 1) * P],
                                       ml[:, t, :, :].rearrange("p a i -> p (a i)"), ident[:, :])
                ins.then_inc(rows_T, 1)

            def score_exp(T, t, slot, hf, early):
                if hf == 0 and not early:
                    pe.wait_ge(exp_done, T - 1)
                k, i = (t % 32) // REP, t % REP
                ins = pe.matmul(PS[:, B_EXP + 2 * (t % 2) + hf, :], kst[0:98, slot, k * P:(k + 1) * P],
                                qst[0:98, slot, i, hf * 512:(hf + 1) * 512], start=True, stop=True)
                if hf == 1:
                    ins.then_inc(exp_in, 1)

            def values(T, t, slot, hf):
                if hf == 0:
                    pe.wait_ge(exp_done, T + 1)
                k, i = (t % 32) // REP, t % REP
                ins = pe.matmul(PS[32 * i:32 * i + 32, B_OUT + hf, :], vst[:, slot, k, :],
                                pex[:, t % NP_BUF, hf * 512:(hf + 1) * 512], start=(k == 0),
                                stop=(k == QT - 1))
                if hf == 1:
                    ins.then_inc(pv_done, 1)

            def transpose_outputs(u):
                pe.wait_ge(o_sb, u + 1)
                for t in range(QT):
                    ins = pe.transpose(PS[:, B_MAX + t // 4, (t % 4) * P:(t % 4 + 1) * P],
                                       oT[:, t * P:(t + 1) * P], identf[:, :])
                ins.then_inc(o_T, 1)

            def transpose_tokens(v):
                for h in range(2):
                    pe.wait_ge(o_split, 2 * v + h + 1)
                    for t in range(QT):
                        ins = pe.transpose(bank16(B_MAX + h)[:, t * P:(t + 1) * P],
                                           osp[h][:, t * P:(t + 1) * P], ident[:, :])
                    ins.then_inc(oT_done, 1)

            def project_outputs(v, kk, rnd):
                if rnd == 0:
                    pe.wait_ge(oT_sb, 2 * v + 2)
                else:
                    pe.wait_ge(xo_done, 2 * v + 1)
                for i in range(4):
                    t = rnd * 4 + i
                    for m, (b, a) in enumerate(PASSES):
                        ins = pe.matmul(PS[:, B_MAX + i // 2, (i % 2) * HID:(i % 2 + 1) * HID],
                                        oTT[a][:, t * P:(t + 1) * P],
                                        WO[b][:, kk, :].rearrange("p a n -> p (a n)"),
                                        start=(m == 0 and i % 2 == 0), stop=(m == 2), skip_group_check=True)
                ins.then_inc(yo_done, 1)

            def pair(v, first, last):
                for w in range(2):
                    u = 2 * v + w
                    pe.wait_ge(rows_in[w], 128 * (v + 1))
                    for t in range(32):
                        T, tt = u * 32 + t, w * 32 + t
                        more = not (last and w == 1)
                        if more and t == MAX_FROM:
                            pe.wait_ge(q_in[1 - w], 96 * (v + w + 1))
                            if not (first and w == 0):
                                pe.wait_ge(o_norm, u)
                        for quarter in range(4):
                            if more:
                                score_max(u + 1, 1 - w, max_parts(t, quarter))
                            if quarter < 2:
                                score_exp(T, tt, w, quarter, first and w == 0 and t < 2)
                            elif t >= LAG:
                                if t == LAG and quarter == 2:
                                    pe.wait_ge(v_in[w], 16 * (v + 1))
                                    if not (first and w == 0):
                                        pe.wait_ge(o_sb, u)
                                values(T - LAG, tt - LAG, w, quarter - 2)
                            elif not (first and w == 0):
                                values(T - LAG, (tt - LAG) % 64, 1 - w, quarter - 2)
                        if more and t == MAX_TO:
                            transpose_max(u + 1)
                        if w == 1 and not first and t == 0:
                            pe.wait_ge(rows_sb, u + 1)
                            transpose_tokens(v - 1)
                        if w == 1 and not first and t in (1, 2):
                            project_outputs(v - 1, bass.ds((v - 1) % 2, 1), t - 1)
                        if t == LAG and not (first and w == 0):
                            if w == 1 and not first:
                                pe.wait_ge(xo_done, 2 * v)
                            else:
                                pe.wait_ge(rows_sb, u + 1)
                            transpose_outputs(u - 1)

            pe.wait_ge(q_in[0], 96)
            pe.wait_ge(const_rows, 1)
            score_max(0, 0, range(64), True)
            transpose_max(0)
            pair(0, True, False)
            with pe.Fori(1, UNITS // 2 - 1) as v:
                pair(v, False, False)
            v = UNITS // 2 - 1
            pair(v, False, True)
            for t in range(64 - LAG, 64):
                for hf in range(2):
                    values(v * 64 + t, t, 1, hf)
            pe.wait_ge(o_norm, UNITS - 1)
            transpose_outputs(UNITS - 1)
            pe.wait_ge(o_norm, UNITS)
            transpose_tokens(v)
            for rnd in range(2):
                project_outputs(v, bass.ds(v % 2, 1), rnd)
            pe.wait_ge(xo_done, UNITS)

            layer(L[1], N[2], R[1], None)


def rope_tables():
    inv = (np.float32(1.0) / np.float32(10000.0) ** (np.arange(0, HD, 2, dtype=np.float32) / np.float32(HD)))
    ang = np.arange(SEQ, dtype=np.float32)[:, None] * inv.astype(np.float32)[None, :]
    ang = np.concatenate([ang, ang], axis=-1)
    cos, sin = np.cos(ang).T.astype(np.float32), np.sin(ang).T.astype(np.float32)
    sin = np.concatenate([-sin[:HD // 2], sin[HD // 2:]])
    qtab = np.tile(np.concatenate([cos, sin]), (4, 1))
    ktab = np.stack([np.tile(cos, (8, 1)), np.tile(sin, (8, 1))])
    return np.ascontiguousarray(qtab), np.ascontiguousarray(ktab)


def layouts(a):
    swap = (np.arange(HD) + HD // 2) % HD

    def on_partitions(w):
        return np.ascontiguousarray(w.T.reshape(KT, P, -1).transpose(1, 0, 2).reshape(P, -1))

    gup = a["L0_ffn_gate_up_proj"]
    gate, upw = gup[:, :INTER, :].reshape(-1, HID), gup[:, INTER:, :].reshape(-1, HID)
    down = a["L0_ffn_down_proj"].transpose(0, 2, 1).reshape(CHUNKS, P, HID)
    q = a["L0_attn_Wq"].reshape(HEADS, HD, HID)
    k = a["L0_attn_Wk"].reshape(KV, HD, HID)
    return {
        "x": a["L0_attn_x"].reshape(TOKENS, HID),
        "wgu": on_partitions(np.concatenate([gate, upw])),
        "wd": np.ascontiguousarray(down.transpose(1, 0, 2).reshape(P, -1)),
        "wg": on_partitions(a["L0_ffn_gate_weight"]),
        "wq": on_partitions(np.concatenate([q, q[:, swap]], axis=1).reshape(-1, HID)),
        "wk": on_partitions(np.concatenate([np.concatenate([k, k], axis=1),
                                            np.concatenate([k[:, swap], k[:, swap]], axis=1)]).reshape(-1, HID)),
        "wv": on_partitions(a["L0_attn_Wv"]),
        "wo": on_partitions(a["L0_attn_Wo"]),
    }


def constants():
    owner = np.arange(CHUNKS * P) // INTER
    sel = (np.arange(3 * EXPERTS)[:, None] % EXPERTS == owner[None, :]).astype(np.float16)
    qtab, ktab = rope_tables()
    return {"sel_c": sel.reshape(3 * EXPERTS, CHUNKS, P), "ident_c": np.eye(P, dtype=np.float16),
            "qtab_c": qtab, "ktab_c": ktab}


def kernel(**inputs):
    import concourse.bacc as bacc
    from concourse.bass_utils import run_bass_kernel_spmd

    arrays = {**layouts({k: np.asarray(v) for k, v in inputs.items()}), **constants()}
    nc = bacc.Bacc("TRN2", target_bir_lowering=False, num_devices=1)
    args = {k: nc.dram_tensor(k, v.shape, mybir.dt.from_np(v.dtype), kind="ExternalInput").ap()
            for k, v in arrays.items()}
    out = nc.dram_tensor("out", (TOKENS, HID), F32, kind="ExternalOutput").ap()
    build(nc, **args, out=out)
    r = run_bass_kernel_spmd(nc, [arrays], core_ids=[0])
    return r.results[0]["out"].reshape(BATCH, SEQ, HID)
```
